# Optimizing a Trainium2 kernel written in Bass

```python
import numpy as np
import jax
import jax.numpy as jnp

def _softmax(x, axis=-1):
    return jax.nn.softmax(x, axis=axis)

def _gelu(x):
    return jax.nn.gelu(x, approximate=True)

def _silu(x):
    return jax.nn.silu(x)

def _sigmoid(x):
    return jax.nn.sigmoid(x)

def _layernorm(x, axis=-1, eps=1e-05):
    m = jnp.mean(x, axis=axis, keepdims=True)
    v = jnp.var(x, axis=axis, keepdims=True)
    return (x - m) / jnp.sqrt(v + eps)

def _scatter_add(tgt, idx, src, axis=0):
    return tgt.at[idx].add(src)

def _segment_sum(src, seg, n):
    return jax.ops.segment_sum(src, seg, n)
kernel_name = 'mk_gnn_resnorm_d1_gnn_r32_26100f'

def setup_inputs(seed: int=0):
    np.random.seed(seed)
    _w = jnp.asarray

    def _rec_inputs():
        import jax
        import jax.numpy as jnp
        _gk = jax.random.key(seed)
        x = -0.000202 + 1 * jax.random.normal(jax.random.fold_in(_gk, 1), (3125, 64), jnp.float32)
        _s = jax.random.randint(jax.random.fold_in(_gk, 2), (50000,), 0, 3125, jnp.int32)
        _d = jax.random.randint(jax.random.fold_in(_gk, 3), (50000,), 0, 3125, jnp.int32)
        _loop = jnp.arange(3125, dtype=jnp.int32)
        src = jnp.concatenate([_s, _d, _loop])
        dst = jnp.concatenate([_d, _s, _loop])
        _o = jnp.argsort(dst, stable=True)
        src = src[_o]
        dst = dst[_o]
        edge_attr_32 = -5.16925e-05 + 1.00005 * jax.random.normal(jax.random.fold_in(_gk, 12), (103125, 32), jnp.float32)
        return (x, src, dst, edge_attr_32)
    x, src, dst, edge_attr_32 = _rec_inputs()

    def _L0_gnn_setup():
        import jax, jax.numpy as jnp
        import numpy as np
        N_NODES = 3125
        N_EDGES = 100000
        EDGE_OUT = 32
        HID = 128
        NODE_OUT = 64
        N_GRAPHS = 16
        key = jax.random.key(seed)
        ks = jax.random.split(key, 9)
        x = jax.random.normal(ks[0], (N_NODES, 64), dtype=jnp.float32)
        edge_index = jax.random.randint(ks[1], (2, N_EDGES), 0, N_NODES, dtype=jnp.int64)
        edge_attr = jax.random.normal(ks[2], (N_EDGES, EDGE_OUT), dtype=jnp.float32)
        u = jax.random.normal(ks[3], (N_GRAPHS, 1), dtype=jnp.float32)
        batch = jnp.sort(jax.random.randint(ks[4], (N_NODES,), 0, N_GRAPHS, dtype=jnp.int64))
        d_in = 3 * EDGE_OUT + 1
        W1 = jax.random.normal(ks[5], (d_in, HID), dtype=jnp.float32) / np.sqrt(d_in)
        b1 = jnp.zeros((HID,), dtype=jnp.float32)
        W2 = jax.random.normal(ks[6], (HID, NODE_OUT), dtype=jnp.float32) / np.sqrt(HID)
        b2 = jnp.zeros((NODE_OUT,), dtype=jnp.float32)
        return {'x': x, 'edge_index': edge_index, 'edge_attr': edge_attr, 'u': u, 'batch': batch, 'W1': W1, 'b1': b1, 'W2': W2, 'b2': b2}
    _L0_gnn_all = _L0_gnn_setup()
    _L0_gnn_in = {k: v for k, v in _L0_gnn_all.items() if k in ('u', 'W1', 'b1', 'W2', 'b2')}
    del _L0_gnn_all
    return {'x': x, 'src': src, 'dst': dst, 'edge_attr_32': edge_attr_32, 'L0_gnn_u': _L0_gnn_in['u'], 'L0_gnn_W1': _L0_gnn_in['W1'], 'L0_gnn_b1': _L0_gnn_in['b1'], 'L0_gnn_W2': _L0_gnn_in['W2'], 'L0_gnn_b2': _L0_gnn_in['b2']}

def reference(x, src, dst, edge_attr_32, L0_gnn_u, L0_gnn_W1, L0_gnn_b1, L0_gnn_W2, L0_gnn_b2):
    import jax
    import jax.numpy as jnp

    def _L0_gnn_ref(x, edge_index, edge_attr, u, batch, W1, b1, W2, b2):
        import jax, jax.numpy as jnp
        import numpy as np
        N_NODES = 3125
        N_EDGES = 100000
        EDGE_OUT = 32
        HID = 128
        NODE_OUT = 64
        N_GRAPHS = 16
        N = x.shape[0]
        row = edge_index[0]
        seg_sum = jax.ops.segment_sum(edge_attr, row, num_segments=N)
        seg_max = jax.ops.segment_max(edge_attr, row, num_segments=N)
        cnt = jax.ops.segment_sum(jnp.ones((edge_attr.shape[0], 1), edge_attr.dtype), row, num_segments=N)
        seg_mean = seg_sum / jnp.maximum(cnt, 1.0)
        seg_max = jnp.where(cnt > 0, seg_max, 0.0)
        h = jnp.concatenate([seg_sum, seg_max, seg_mean, u[batch]], axis=1)
        h = jax.nn.relu(h @ W1 + b1)
        return h @ W2 + b2
    edge_index = jnp.stack([src, dst])
    batch0 = jnp.zeros((3125,), jnp.int32)
    x = _layernorm(x + _L0_gnn_ref(x, edge_index, edge_attr_32, L0_gnn_u, batch0, L0_gnn_W1, L0_gnn_b1, L0_gnn_W2, L0_gnn_b2), axis=-1)
    return x

_drawn_inputs = setup_inputs


def setup_inputs(seed=0):
    import zlib

    import numpy as np

    out = dict(_drawn_inputs(seed))
    spreads = {'L0_gnn_b1': (0.0, 0.278), 'L0_gnn_b2': (0.0, 0.1)}
    factors = {'L0_gnn_u': 2.897}
    for name, (base, spread) in spreads.items():
        noise = np.random.default_rng([zlib.crc32(name.encode()), seed]).standard_normal(out[name].shape)
        drawn = base * np.exp(spread * noise) if base else spread * noise
        out[name] = jnp.asarray(drawn.astype(out[name].dtype))
    for name, factor in factors.items():
        out[name] = (out[name] * factor).astype(out[name].dtype)
    return out
```

```python
import concourse.bass as bass
from concourse import mybir
from contextlib import ExitStack

F32 = mybir.dt.float32
BF16 = mybir.dt.bfloat16
F16 = mybir.dt.float16
I32 = mybir.dt.int32
U32 = mybir.dt.uint32
ALU = mybir.AluOpType
ACT = mybir.ActivationFunctionType
AX = mybir.AxisListType

P = 128
N_NODES = 3125
N_EDGES = 103125
FE = 32
FN = 64
FR = 2 * FE
HID = 128
LO = 33
HI = P - LO
BT = 8
GB = 10
HALF = GB // 2
GT = GB * BT
N_GROUPS = N_EDGES // (P * GT)
N_BATCH = N_GROUPS * GB
MAIN = N_GROUPS * GT
REST = N_EDGES - P * MAIN
REST_T = REST // P
TAIL = REST - P * REST_T
RT = REST_T + (TAIL > 0)
TILES = MAIN + RT
PAD = P * RT - REST
PARTS = [2, 5, 3]
NP_ = len(PARTS)
SLOT = BT + 1
NODE_P = 125
NODE_J = N_NODES // NODE_P
CHUNK = 134
FMAX = 3.4028234663852886e38
ROUND = 12582912.0
EPS = 1e-5
LAG = 2
RING_J = 5

FIRST_GROUP = [sum(PARTS[:s]) for s in range(NP_ + 1)]
M = [PARTS[s] * GT + (RT if s == NP_ - 1 else 0) for s in range(NP_)]
CHUNKS = []
for _m in M:
    _n = -(-_m // CHUNK)
    _step = -(-_m // _n)
    CHUNKS.append([(c * _step, min((c + 1) * _step, _m)) for c in range(_n)])
FIRST_CHUNK = [sum(len(c) for c in CHUNKS[:s]) for s in range(NP_ + 1)]
MMAX = max(M)
EARLY = M[0] + BT

PLAN = [("count", 0), ("place", 0, 10), ("count", 1), ("load", 0), ("place", 10, 13), ("heads", 0), ("place", 13, 15),
        ("scan", 0, 0), ("place", 15, 17), ("scan", 0, 1), ("carry", 0), ("place", 17, 20),
        ("load", 1), ("place", 20, 25), ("mend", 0), ("place", 25, 30), ("count", 2), ("place", 30, 33), ("heads", 1),
        ("place", 33, 35), ("place", 35, 40),
        ("scan", 1, 0), ("place", 40, 42), ("scan", 1, 1), ("place", 42, 45),
        ("scan", 1, 2), ("carry", 1), ("place", 45, 46), ("load", 2), ("place", 46, 47), ("mend", 1),
        ("place", 47, 50), ("rest",), ("heads", 2), ("scan", 2, 0), ("scan", 2, 1), ("carry", 2),
        ("fetched", 0), ("mend", 2), ("fetched", 1)]
POOL_PLAN = [("scatter", 0, 2), ("scatter", 2, 4), ("mend", 0), ("scatter", 4, 5), ("put", 0),
             ("scatter", 5, 7), ("scatter", 7, 9), ("mend", 1), ("scatter", 9, 10),
             ("rest",), ("put", 1), ("fetch", 0, 0, NODE_J), ("fetch", 1, 0, 20), ("mend", 2), ("fetch", 1, 20, NODE_J),
             ("put", 2), ("fetch", 2, 0, NODE_J)]
for _s, _c in enumerate(CHUNKS):
    assert [p[2] for p in PLAN if p[:2] == ("scan", _s)] == list(range(len(_c)))


def gnn_kernel(nc, x, src, edges, u, w1, b1, w2, b2, out):
    sorted_d = [nc.dram_tensor(f"sorted_{s}", [P * M[s], FE], F32, kind="Internal").ap() for s in range(NP_)]
    scanned_d = [nc.dram_tensor(f"scanned_{s}", [P * M[s], FR], F32, kind="Internal").ap() for s in range(NP_)]
    ends_d = [nc.dram_tensor(f"ends_{s}", [HI * LO], F32, kind="Internal").ap() for s in range(NP_)]
    counts_d = [nc.dram_tensor(f"counts_{s}", [HI * LO], F32, kind="Internal").ap() for s in range(NP_)]

    def by_partition(a):
        return a.rearrange("(p n) -> p n", p=NODE_P)

    with ExitStack() as ctx:
        def sb(name, shape, dt=F32):
            return ctx.enter_context(nc.sbuf_tensor(name, shape, dt))

        def bank(name, dt=F32):
            return ctx.enter_context(nc.psum_tensor(name, [P, 512 if dt == F32 else 1024], dt))

        def sem(name):
            return ctx.enter_context(nc.semaphore(name))

        diff = sb("diff", [P, P], I32)
        ramp_i = sb("ramp_i", [P, 512], I32)
        ramp = sb("ramp", [P, 512], F16)
        ramp32 = sb("ramp32", [P, 512])
        ramp_b = sb("ramp_b", [P, HI], BF16)
        row0 = sb("row0", [P, 1], I32)
        row_f = sb("row_f", [P, 1])
        slot_i = sb("slot_i", [P, LO * SLOT], I32)
        keep = sb("keep", [P, LO * SLOT])
        ident = sb("ident", [P, P])
        ident_b = sb("ident_b", [P, P], BF16)
        before = sb("before", [P, P], BF16)
        above = sb("above", [P, P], BF16)
        key_i = sb("key_i", [P, TILES], I32)
        key_f = sb("key_f", [P, TILES])
        hi_f = sb("hi_f", [P, TILES])
        hi_b = sb("hi_b", [P, TILES], BF16)
        lo_b = sb("lo_b", [P, TILES], BF16)
        hot_c = sb("hot_c", [P, 2, BT, P], BF16)
        hot = sb("hot", [P, 2, BT, P], BF16)
        hot_t = sb("hot_t", [P, 2, BT, P], BF16)
        hist = sb("hist", [P, LO])
        incl = sb("incl", [P, LO])
        tot1 = sb("tot1", [P, 1], BF16)
        tot2 = sb("tot2", [P, 1], BF16)
        ends = sb("ends", [P, LO])
        starts = sb("starts", [P, NP_, LO])
        ones_lo = sb("ones_lo", [P, LO])
        steps = sb("steps", [P, 2, LO, SLOT])
        runs = sb("runs", [P, 2, LO, SLOT])
        part1 = sb("part1", [P, 2, LO, SLOT], BF16)
        part2 = sb("part2", [P, 2, LO, SLOT], BF16)
        picked = sb("picked", [P, BT, LO])
        base = sb("base", [P, BT])
        rank = sb("rank", [P, 2, BT])
        rank_of = sb("rank_of", [P, 2, BT, P], BF16)
        place = sb("place", [P, GB, BT], U32)
        rows = sb("rows", [P, GB, BT, FE])
        end_n = sb("end_n", [NODE_P, NP_, NODE_J])
        cnt_n = sb("cnt_n", [NODE_P, NP_, NODE_J])
        has_n = sb("has_n", [NODE_P, NP_, NODE_J])
        cap_n = sb("cap_n", [NODE_P, NP_, NODE_J])
        beg_n = sb("beg_n", [NODE_P, NODE_J])
        hp_n = sb("hp_n", [NODE_P, NODE_J])
        hc_n = sb("hc_n", [NODE_P, NODE_J])
        at_n = sb("at_n", [NODE_P, NP_, NODE_J], U32)
        head_p = sb("head_p", [NODE_P, RING_J, P], BF16)
        head_c = sb("head_c", [NODE_P, RING_J, MMAX], BF16)
        same = sb("same", [P, MMAX])
        cap = sb("cap", [P, MMAX])
        far = sb("far", [P, MMAX])
        first = sb("first", [P, 1])
        mend_f = sb("mend_f", [P, 1])
        limit = sb("limit", [P, NP_])
        mend_at = sb("mend_at", [P, NP_], U32)
        whole = sb("whole", [P, 1])
        links = sb("links", [P, 2, FR], BF16)
        xs = sb("xs", [P, 2, CHUNK, FE])
        rs = sb("rs", [P, 2, CHUNK, FR])
        last = sb("last", [P, FR])
        tails = sb("tails", [FR, P])
        link_a = sb("link_a", [FR, P])
        link_b = sb("link_b", [FR, P])
        full = sb("full", [FR, P])
        carried = sb("carried", [FR, P])
        carry = sb("carry", [P, FR])
        mended = sb("mended", [P, NP_, FR])
        got = sb("got", [NODE_P, 2, NODE_J, FR])
        feat = sb("feat", [NODE_P, NODE_J, 3 * FE])
        cnt_all = sb("cnt_all", [NODE_P, NODE_J])
        cnt_1 = sb("cnt_1", [NODE_P, NODE_J])
        inv = sb("inv", [NODE_P, NODE_J])
        has_all = sb("has_all", [NODE_P, NODE_J])
        w1_s = sb("w1_s", [3 * FE, HID])
        w1_u = sb("w1_u", [1, HID])
        u_s = sb("u_s", [1, 1])
        b1_s = sb("b1_s", [HID, 1])
        bias1 = sb("bias1", [HID, 1])
        w2_s = sb("w2_s", [HID, FN])
        b2_s = sb("b2_s", [1, FN])
        one_row = sb("one_row", [1, P])
        x_s = sb("x_s", [NODE_P, NODE_J, FN])
        COLS = 4 * NODE_P
        NB = -(-NODE_J // 4)
        blocks = [(j, min(j + 4, NODE_J)) for j in range(0, NODE_J, 4)]
        ft = xs[:, :, :, :].rearrange("p a b c -> p (a b c)")[0:3 * FE, 0:2 * COLS].rearrange("p (a b) -> p a b", a=2)
        ht = xs[:, :, :, :].rearrange("p a b c -> p (a b c)")[:, 2 * COLS:4 * COLS].rearrange("p (a b) -> p a b", a=2)
        y = rs[0:NODE_P, 0, 0:NODE_J, :]
        sq = rs[0:NODE_P, 0, NODE_J:2 * NODE_J, :]
        o_s = rs[0:NODE_P, 0, 2 * NODE_J:3 * NODE_J, :]
        mean = sb("mean", [NODE_P, NODE_J])
        var = sb("var", [NODE_P, NODE_J])
        std = sb("std", [NODE_P, NODE_J])
        rstd = sb("rstd", [NODE_P, NODE_J])

        hot_tp = [bank(f"hot_tp{k}", BF16) for k in range(2)]
        match = [bank(f"match{k}") for k in range(2)]
        steps_p = bank("steps_p")
        entry_p = bank("entry_p")
        hist_p = bank("hist_p")
        misc_p = bank("misc_p")

        made = sem("made")
        const_ready = sem("const_ready")
        key_loaded = sem("key_loaded")
        key_tail = sem("key_tail")
        key_first = sem("key_first")
        w_loaded = sem("w_loaded")
        x_loaded = sem("x_loaded")
        dve_step = sem("dve_step")
        c_hot = sem("c_hot")
        c_used = sem("c_used")
        hist_read = sem("hist_read")
        offs_ready = sem("offs_ready")
        table_ready = sem("table_ready")
        table_out = sem("table_out")
        table_in = sem("table_in")
        hot_ready = sem("hot_ready")
        step_cnt = sem("step_cnt")
        hot_tr = sem("hot_tr")
        steps_ready = sem("steps_ready")
        hot_t_ready = sem("hot_t_ready")
        parts_ready = sem("parts_ready")
        match_ready = sem("match_ready")
        rank_ready = sem("rank_ready")
        entry_ready = sem("entry_ready")
        picked_ready = sem("picked_ready")
        place_ready = sem("place_ready")
        rows_in = [sem(f"rows_in{h}") for h in range(2)]
        rest_in = sem("rest_in")
        scat = [sem(f"scat{k}") for k in range(HALF)]
        scattered = sem("scattered")
        begun = sem("begun")
        pad_out = sem("pad_out")
        heads_hot = sem("heads_hot")
        heads_used = sem("heads_used")
        marks_read = sem("marks_read")
        xs_in = [sem(f"xs_in{k}") for k in range(2)]
        scanned = sem("scanned")
        rs_out = [sem(f"rs_out{k}") for k in range(2)]
        last_ready = sem("last_ready")
        tails_ready = sem("tails_ready")
        carried_ready = sem("carried_ready")
        carry_tr = sem("carry_tr")
        carry_ready = sem("carry_ready")
        mend_in = sem("mend_in")
        mend_done = sem("mend_done")
        mend_out = sem("mend_out")
        fetch_in = [sem(f"fetch_in{s}") for s in range(NP_ - 1)]
        fetch_last = [sem(f"fetch_last{k}") for k in range(len(range(0, NODE_J, 4)))]
        got_used = sem("got_used")
        bias_p = sem("bias_p")
        feat_ready = sem("feat_ready")
        ft_p = sem("ft_p")
        ft_ready = sem("ft_ready")
        h_p = sem("h_p")
        h_ready = sem("h_ready")
        y_p = sem("y_p")
        var_ready = sem("var_ready")
        std_ready = sem("std_ready")
        centred = sem("centred")
        sq_ready = sem("sq_ready")
        o_ready = sem("o_ready")
        out_done = sem("out_done")

        def runs_of(kind):
            return [p for p in PLAN if p[0] == kind]

        def batches(s):
            return FIRST_GROUP[s] * GB, FIRST_GROUP[s + 1] * GB, s == NP_ - 1

        class Steps:

            def __init__(self):
                self.n = 0

            def inc(self, ins):
                ins.then_inc(dve_step, 1)
                self.n = self.n + 1

            def wait(self, eng):
                eng.wait_ge(dve_step, self.n)

        block = ctx.enter_context(nc.Block())

        @block.sync
        def _(sp):
            key_main = src[0:P * MAIN].rearrange("(p t) -> p t", p=P)
            sp.dma_start(key_i[:, 0:EARLY], key_main[:, 0:EARLY]).then_inc(key_first, 16)
            sp.dma_start(key_i[:, EARLY:MAIN], key_main[:, EARLY:MAIN]).then_inc(key_loaded, 16)
            sp.dma_start(key_i[:, MAIN:MAIN + REST_T],
                         src[P * MAIN:N_EDGES - TAIL].rearrange("(p t) -> p t", p=P)).then_inc(key_loaded, 16)
            sp.wait_ge(made, 1)
            sp.dma_start(key_i[0:TAIL, TILES - 1:TILES],
                         src[N_EDGES - TAIL:N_EDGES].rearrange("(p t) -> p t", t=1)).then_inc(key_tail, 16)

            edge_main = edges[0:P * MAIN, :].rearrange("(p t) f -> p (t f)", p=P)

            def load_rows(g):
                for h in range(2):
                    if not (isinstance(g, int) and g == 0):
                        sp.wait_ge(scattered, g * GB - GB + HALF * h + HALF)
                    n = HALF * BT * FE
                    sp.dma_start(rows[:, HALF * h:HALF * h + HALF, :, :].rearrange("p a b c -> p (a b c)"),
                                 edge_main[:, bass.ds(g * (2 * n) + h * n, n)]).then_inc(rows_in[h], 16)

            load_rows(0)
            sp.dma_start(w1_s[:, :], w1[0:3 * FE, :]).then_inc(w_loaded, 16)
            sp.dma_start(w1_u[:, :], w1[3 * FE:3 * FE + 1, :]).then_inc(w_loaded, 16)
            sp.dma_start(u_s[:, :], u[0:1, :]).then_inc(w_loaded, 16)
            sp.dma_start(b1_s[:, :], b1.rearrange("(p a) -> p a", a=1)).then_inc(w_loaded, 16)
            sp.dma_start(w2_s[:, :], w2).then_inc(w_loaded, 16)
            sp.dma_start(b2_s[:, :], b2.rearrange("(a n) -> a n", a=1)).then_inc(w_loaded, 16)
            sp.dma_start(x_s[:, :, :].rearrange("p a b -> p (a b)"),
                         x.rearrange("(p j) f -> p (j f)", p=NODE_P)).then_inc(x_loaded, 16)

            def load_chunk(s, c):
                k = FIRST_CHUNK[s] + c
                if c == 0:
                    sp.wait_ge(scattered, batches(s)[1] + (s == NP_ - 1))
                    if s == NP_ - 1:
                        sp.wait_ge(pad_out, 16)
                if k >= 2:
                    sp.wait_ge(scanned, k - 1)
                a, b = CHUNKS[s][c]
                sp.dma_start(xs[:, k % 2, 0:b - a, :].rearrange("p a b -> p (a b)"),
                             sorted_d[s].rearrange("(p m) f -> p (m f)", p=P)[:, a * FE:b * FE]).then_inc(xs_in[k % 2], 16)

            for s in range(NP_):
                g0, g1 = FIRST_GROUP[s], FIRST_GROUP[s + 1]
                lo_g = 1 if s == 0 else g0 + 1
                hi_g = min(g1 + 1, N_GROUPS)
                if hi_g > lo_g:
                    with sp.Fori(lo_g, hi_g) as g:
                        load_rows(g)
                if s == NP_ - 1:
                    sp.wait_ge(scattered, N_BATCH - GB + 1)
                    sp.dma_start(rows[:, 0, 0:REST_T, :].rearrange("p a b -> p (a b)"),
                                 edges[P * MAIN:N_EDGES - TAIL, :].rearrange("(p t) f -> p (t f)", p=P)).then_inc(rest_in, 16)
                    sp.dma_start(rows[0:TAIL, 0, REST_T, :], edges[N_EDGES - TAIL:N_EDGES, :]).then_inc(rest_in, 16)
                for c in range(len(CHUNKS[s])):
                    load_chunk(s, c)

            cuts = [0, NB - 2, NB]
            for k in range(2):
                a, b = blocks[cuts[k]][0], blocks[cuts[k + 1] - 1][1]
                sp.wait_ge(o_ready, cuts[k + 1])
                sp.dma_start(out.rearrange("(p j) f -> p j f", p=NODE_P)[:, a:b, :], o_s[:, a:b, :]).then_inc(out_done, 16)
            sp.wait_ge(out_done, 32)

        @block.gpsimd
        def _(pool):
            pool.memset(key_i[:, TILES - 1:TILES], N_NODES).then_inc(made, 1)
            pool.iota(ramp_i[:, :], pattern=[[1, 512]], base=0, channel_multiplier=0).then_inc(made, 1)
            pool.iota(diff[:, :], pattern=[[1, P]], base=0, channel_multiplier=-1).then_inc(made, 1)
            pool.iota(row0[:, :], pattern=[[0, 1]], base=0, channel_multiplier=1).then_inc(made, 1)
            pool.iota(slot_i[:, :], pattern=[[0, LO], [1, SLOT]], base=0, channel_multiplier=0).then_inc(made, 1)

            def scatter_tile(s, slot, t, n):
                pool.indirect_dma_start(
                    out=sorted_d[s], out_offset=bass.IndirectOffsetOnAxis(ap=place[0:n, slot, t:t + 1], axis=0),
                    in_=rows[0:n, slot, t, :], in_offset=None).then_inc(scat[slot % HALF], 16)

            def retire(g, k, tiles=BT):
                pool.wait_ge(scat[k % HALF], (g * 2 + k // HALF) * (16 * BT) + 16 * tiles)
                pool.sem_inc(scattered, 1)

            def scatter_group(s, g, at_start=False):
                for k in range(GB):
                    b = g * GB + k
                    pool.wait_ge(place_ready, b + 1)
                    if k % HALF == 0:
                        pool.wait_ge(rows_in[k // HALF], g * 16 + 16)
                    pool.sem_inc(begun, 1)
                    for t in range(BT):
                        scatter_tile(s, k, t, P)
                    if k >= LAG:
                        retire(g, k - LAG)
                    elif not at_start:
                        retire(g - 1, GB + k - LAG)

            def mend_rows(s):
                k0, k1 = FIRST_CHUNK[s], FIRST_CHUNK[s + 1]
                pool.wait_ge(carry_ready, s + 1)
                for par in range(2):
                    n = len([k for k in range(k1) if k % 2 == par])
                    if n:
                        pool.wait_ge(rs_out[par], 16 * n)
                pool.indirect_dma_start(
                    out=mended[:, s, :], out_offset=None, in_=scanned_d[s],
                    in_offset=bass.IndirectOffsetOnAxis(ap=mend_at[:, s:s + 1], axis=0)).then_inc(mend_in, 16)

            def put_rows(s):
                pool.wait_ge(mend_done, s + 1)
                pool.indirect_dma_start(
                    out=scanned_d[s], out_offset=bass.IndirectOffsetOnAxis(ap=mend_at[:, s:s + 1], axis=0),
                    in_=mended[:, s, :], in_offset=None).then_inc(mend_out, 16)

            def fetch_nodes(s, j0, j1):
                if j0 == 0:
                    pool.wait_ge(mend_out, 16 * (s + 1))
                if s >= 2 and j0 == 0:
                    pool.wait_ge(got_used, s - 1)
                for j in range(j0, j1):
                    pool.indirect_dma_start(
                        out=got[:, s % 2, j, :], out_offset=None, in_=scanned_d[s],
                        in_offset=bass.IndirectOffsetOnAxis(ap=at_n[:, s, j:j + 1], axis=0)).then_inc(
                            fetch_last[j // 4] if s == NP_ - 1 else fetch_in[s], 16)

            for step in POOL_PLAN:
                if step[0] == "scatter":
                    part = max(s for s in range(NP_) if FIRST_GROUP[s] <= step[1])
                    if step[1] == 0:
                        scatter_group(part, 0, at_start=True)
                    if step[2] > 1:
                        with pool.Fori(max(step[1], 1), step[2]) as g:
                            scatter_group(part, g)
                elif step[0] == "rest":
                    pool.wait_ge(place_ready, N_BATCH + 1)
                    pool.wait_ge(rest_in, 32)
                    for t in range(RT):
                        scatter_tile(NP_ - 1, 0, t, P if t < REST_T else TAIL)
                    for k in range(GB - LAG, GB):
                        retire(N_GROUPS - 1, k)
                    retire(N_GROUPS, 0, RT)
                elif step[0] == "mend":
                    mend_rows(step[1])
                elif step[0] == "put":
                    put_rows(step[1])
                elif step[0] == "fetch":
                    fetch_nodes(*step[1:])

        @block.scalar
        def _(act):
            def copy_batch(b, par, nt=BT):
                act.wait_ge(step_cnt, b + 1)
                if not (isinstance(b, int) and b < 2):
                    act.wait_ge(parts_ready, b - 1)
                nc.scalar.copy(steps[0:HI, par, :, 1:1 + nt],
                               steps_p[0:HI, 0:LO * BT].rearrange("p (l t) -> p l t", t=BT)[:, :, 0:nt]).then_inc(steps_ready, 1)
                act.wait_ge(hot_tr, b + 1)
                if not (isinstance(b, int) and b < 2):
                    act.wait_ge(entry_ready, b - 1)
                nc.scalar.copy(hot_t[:, par, 0:nt, :].rearrange("p a b -> p (a b)"),
                               hot_tp[par][:, 0:nt * P]).then_inc(hot_t_ready, 1)

            def rank_batch(b, par, nt=BT):
                if not (isinstance(b, int) and b < 2):
                    act.wait_ge(place_ready, b - 1)
                for h in range(2):
                    act.wait_ge(match_ready, b * 2 + h + 1)
                    for t in range(h * BT // 2, min((h + 1) * BT // 2, nt)):
                        ins = nc.scalar.activation(rank_of[:, par, t, :], match[h][:, (t % (BT // 2)) * P:(t % (BT // 2) + 1) * P],
                                                   ACT.Relu, accum_out=rank[:, par, t:t + 1])
                    ins.then_inc(rank_ready, 1)

            started = False
            for step in PLAN:
                if step[0] == "count":
                    s = step[1]
                    act.wait_ge(table_ready, s + 1)
                    act.dma_start(ends_d[s].rearrange("(p n) -> p n", p=HI), ends[0:HI, :]).then_inc(table_out, 16)
                    act.dma_start(counts_d[s].rearrange("(p n) -> p n", p=HI), hist[0:HI, :]).then_inc(table_out, 16)
                    if s == NP_ - 1:
                        act.wait_ge(bias_p, 2)
                        nc.scalar.activation(bias1[:, :], hist_p[:, 200:201], ACT.Identity, bias=b1_s[:, 0:1]).then_inc(h_ready, 1)
                elif step[0] == "load":
                    s = step[1]
                    act.wait_ge(table_out, 32 * (s + 1))
                    act.dma_start(end_n[:, s, :], by_partition(ends_d[s][0:N_NODES])).then_inc(table_in, 16)
                    act.dma_start(cnt_n[:, s, :], by_partition(counts_d[s][0:N_NODES])).then_inc(table_in, 16)
                elif step[0] == "place":
                    if not started:
                        started = True
                        copy_batch(0, 0)

                    def pair(b0, short_next=False):
                        for par in range(2):
                            rank_batch(b0 + par, par)
                            copy_batch(b0 + par + 1, 1 - par, RT if short_next and par else BT)
                    first_b, last_b = 2 * step[1], 2 * step[2]
                    if first_b == 0:
                        pair(0)
                        first_b = 2
                    short = last_b == N_BATCH
                    with act.Fori(first_b, last_b - 2 * short, 2) as b:
                        pair(b)
                    if short:
                        pair(N_BATCH - 2, short_next=True)
                elif step[0] == "rest":
                    rank_batch(N_BATCH, 0, RT)
                elif step[0] == "scan":
                    s, c = step[1], step[2]
                    k = FIRST_CHUNK[s] + c
                    a, b = CHUNKS[s][c]
                    act.wait_ge(scanned, k + 1)
                    act.dma_start(scanned_d[s].rearrange("(p m) f -> p (m f)", p=P)[:, a * FR:b * FR],
                                  rs[:, k % 2, 0:b - a, :].rearrange("p a b -> p (a b)")).then_inc(rs_out[k % 2], 16)
                elif step[0] == "carry" and step[1] == 0:
                    act.wait_ge(const_ready, 2)
                    act.dma_start(sorted_d[NP_ - 1][P * M[NP_ - 1] - PAD:P * M[NP_ - 1], :],
                                  ramp32[0:PAD, 0:FE]).then_inc(pad_out, 16)
            for k in range(NB + 3):
                if 0 <= k - 3 < NB:
                    a, b = blocks[k - 3]
                    act.wait_ge(var_ready, k - 2)
                    nc.scalar.activation(std[:, a:b], var[:, a:b], ACT.Sqrt).then_inc(std_ready, 1)
                if 0 <= k - 2 < NB:
                    a, b = blocks[k - 2]
                    act.wait_ge(centred, k - 1)
                    nc.scalar.activation(sq[:, a:b, :], y[:, a:b, :], ACT.Square).then_inc(sq_ready, 1)
                if 0 <= k - 1 < NB:
                    q = k - 1
                    n = (blocks[q][1] - blocks[q][0]) * NODE_P
                    act.wait_ge(h_p, q + 1)
                    if q >= 2:
                        act.wait_ge(y_p, q - 1)
                    nc.scalar.activation(ht[:, q % 2, 0:n], match[q % 2][:, 0:n], ACT.Relu,
                                         bias=bias1[:, 0:1]).then_inc(h_ready, 1)
                if k < NB:
                    a, b = blocks[k]
                    n = (b - a) * NODE_P
                    act.wait_ge(ft_p, k + 1)
                    if k >= 2:
                        act.wait_ge(h_p, k - 1)
                    nc.scalar.copy(ft[:, k % 2, 0:n], [misc_p, hist_p][k % 2][0:3 * FE, 0:n]).then_inc(ft_ready, 1)

        @block.tensor
        def _(pe):
            def count_batch(a, par, nt, first, final):
                pe.wait_ge(c_hot, a + 1)
                for t in range(nt):
                    ins = nc.tensor.matmul(hist_p[0:HI, 0:LO], hot_c[:, par, t, 0:HI], hot_c[:, par, t, HI:P],
                                           start=first and t == 0, stop=final and t == nt - 1)
                ins.then_inc(c_used, 1)

            def turn_batch(b, par, nt=BT):
                pe.wait_ge(hot_ready, b + 1)
                if not (isinstance(b, int) and b < 1):
                    pe.wait_ge(steps_ready, b)
                by_tile = steps_p[0:HI, 0:LO * BT].rearrange("p (l t) -> p l t", t=BT)
                for t in range(nt):
                    ins = nc.tensor.matmul(by_tile[:, :, t], hot[:, par, t, 0:HI], hot[:, par, t, HI:P],
                                           start=True, stop=True)
                ins.then_inc(step_cnt, 1)
                if not (isinstance(b, int) and b < 2):
                    pe.wait_ge(hot_t_ready, b - 1)
                for t in range(nt):
                    ins = nc.tensor.transpose(hot_tp[par][:, t * P:(t + 1) * P], hot[:, par, t, :], ident_b[:, :])
                ins.then_inc(hot_tr, 1)

            def match_batch(b, par, nt=BT):
                pe.wait_ge(hot_t_ready, b + 1)
                for h in range(2):
                    if not (isinstance(b, int) and b < 1):
                        pe.wait_ge(rank_ready, b * 2 + h - 1)
                    for t in range(h * BT // 2, min((h + 1) * BT // 2, nt)):
                        o = match[h][:, (t % (BT // 2)) * P:(t % (BT // 2) + 1) * P]
                        nc.tensor.matmul(o, hot_t[:, par, t, :], hot_t[:, par, t, :], start=True, stop=False)
                        ins = nc.tensor.matmul(o, ident_b[:, :], before[:, :], start=False, stop=True)
                    ins.then_inc(match_ready, 1)
                pe.wait_ge(parts_ready, b + 1)
                if not (isinstance(b, int) and b < 1):
                    pe.wait_ge(picked_ready, b)
                for t in range(nt):
                    o = entry_p[:, t * LO:(t + 1) * LO]
                    nc.tensor.matmul(o, hot_t[0:HI, par, t, :], part1[0:HI, par, :, t], start=True, stop=False)
                    ins = nc.tensor.matmul(o, hot_t[0:HI, par, t, :], part2[0:HI, par, :, t], start=False, stop=True)
                ins.then_inc(entry_ready, 1)

            started = False
            rings = 0
            for step in PLAN:
                if step[0] == "count":
                    s = step[1]
                    a0, a1, short = batches(s)
                    if s >= 1:
                        pe.wait_ge(table_ready, s)
                    count_batch(a0, 0, BT, True, False)
                    count_batch(a0 + 1, 1, BT, False, False)
                    if not short:
                        a1 -= 2
                    with pe.Fori(a0 + 2, a1, 2) as a:
                        count_batch(a, 0, BT, False, False)
                        count_batch(a + 1, 1, BT, False, False)
                    if short:
                        count_batch(a1, 0, RT, False, True)
                    else:
                        count_batch(a1, 0, BT, False, False)
                        count_batch(a1 + 1, 1, BT, False, True)
                    pe.wait_ge(hist_read, s + 1)
                    pe.wait_ge(const_ready, 1 + (s > 0))
                    nc.tensor.matmul(hist_p[0:HI, 64:65], above[0:HI, 0:HI], tot1[0:HI, :], start=True, stop=False)
                    nc.tensor.matmul(hist_p[0:HI, 64:65], above[0:HI, 0:HI], tot2[0:HI, :],
                                     start=False, stop=True).then_inc(offs_ready, 1)
                    if s == NP_ - 1:
                        pe.wait_ge(w_loaded, 96)
                        pe.wait_ge(table_ready, NP_)
                        nc.tensor.matmul(hist_p[:, 200:201], w1_u[:, :], u_s[:, :], start=True, stop=True).then_inc(bias_p, 1)
                        nc.tensor.matmul(hist_p[0:NODE_P, 128:128 + FN], one_row[:, 0:NODE_P], b2_s[:, :],
                                         start=True, stop=True).then_inc(bias_p, 1)
                elif step[0] == "place":
                    if not started:
                        started = True
                        turn_batch(0, 0)

                    def pair(b0, short_next=False):
                        for par in range(2):
                            match_batch(b0 + par, par)
                            turn_batch(b0 + par + 1, 1 - par, RT if short_next and par else BT)
                    first_b, last_b = 2 * step[1], 2 * step[2]
                    if first_b == 0:
                        pair(0)
                        first_b = 2
                    short = last_b == N_BATCH
                    with pe.Fori(first_b, last_b - 2 * short, 2) as b:
                        pair(b)
                    if short:
                        pair(N_BATCH - 2, short_next=True)
                elif step[0] == "rest":
                    match_batch(N_BATCH, 0, RT)
                elif step[0] == "heads":
                    s = step[1]
                    if s >= 1:
                        pe.wait_ge(carry_ready, s)
                    for j in range(NODE_J):
                        if j % RING_J == 0:
                            rings += 1
                            pe.wait_ge(heads_hot, rings)
                        ins = nc.tensor.matmul(misc_p[:, 0:M[s]], head_p[:, j % RING_J, :], head_c[:, j % RING_J, 0:M[s]],
                                               start=j == 0, stop=j == NODE_J - 1)
                        if j % RING_J == RING_J - 1:
                            ins.then_inc(heads_used, 1)
                elif step[0] == "carry":
                    s = step[1]
                    pe.wait_ge(last_ready, s + 1)
                    nc.tensor.transpose(misc_p[0:FR, 0:P], last[:, :], ident[:, :])
                    for k in range(2):
                        ins = nc.tensor.matmul(misc_p[0:FR, (k + 1) * P:(k + 2) * P], links[:, k, :], ident_b[:, :],
                                               start=True, stop=True)
                    ins.then_inc(tails_ready, 1)
                    pe.wait_ge(carried_ready, s + 1)
                    nc.tensor.transpose(misc_p[:, 3 * P:3 * P + FR], carried[:, :], ident[0:FR, 0:FR]).then_inc(carry_tr, 1)
            pe.wait_ge(carry_ready, NP_)
            pe.wait_ge(h_ready, 1)
            y_banks = [steps_p, entry_p]
            for k in range(NB + 2):
                if k >= 2:
                    q = k - 2
                    a, b = blocks[q]
                    pe.wait_ge(h_ready, q + 2)
                    if q >= 2:
                        pe.wait_ge(centred, q - 1)
                    for j in range(a, b):
                        ins = nc.tensor.matmul(y_banks[q % 2][0:NODE_P, (j - a) * FN:(j - a + 1) * FN],
                                               ht[:, q % 2, (j - a) * NODE_P:(j - a + 1) * NODE_P], w2_s[:, :],
                                               start=True, stop=True)
                    ins.then_inc(y_p, 1)
                if 1 <= k <= NB:
                    q = k - 1
                    n = (blocks[q][1] - blocks[q][0]) * NODE_P
                    pe.wait_ge(ft_ready, q + 1)
                    if q >= 2:
                        pe.wait_ge(h_ready, q)
                    nc.tensor.matmul(match[q % 2][:, 0:n], w1_s[:, :], ft[:, q % 2, 0:n],
                                     start=True, stop=True).then_inc(h_p, 1)
                if k < NB:
                    a, b = blocks[k]
                    pe.wait_ge(feat_ready, k + 1)
                    if k >= 2:
                        pe.wait_ge(ft_ready, k - 1)
                    for j in range(a, b):
                        ins = nc.tensor.transpose([misc_p, hist_p][k % 2][0:3 * FE, (j - a) * NODE_P:(j - a + 1) * NODE_P],
                                                  feat[:, j, :], ident[0:NODE_P, 0:NODE_P])
                    ins.then_inc(ft_p, 1)

        @block.vector
        def _(dve):
            v = nc.vector
            st = Steps()

            def one_hots(dst, c, nt):
                v.tensor_tensor(dst[:, 0:nt, 0:HI], ramp_b[:, 0:HI].unsqueeze(1).to_broadcast([P, nt, HI]),
                                hi_b[:, bass.ds(c, nt)].unsqueeze(2).to_broadcast([P, nt, HI]), ALU.is_equal)
                return v.tensor_tensor(dst[:, 0:nt, HI:P], ramp_b[:, 0:LO].unsqueeze(1).to_broadcast([P, nt, LO]),
                                       lo_b[:, bass.ds(c, nt)].unsqueeze(2).to_broadcast([P, nt, LO]), ALU.is_equal)

            def count_batch(a, par, nt=BT):
                if not (isinstance(a, int) and a < 2):
                    dve.wait_ge(c_used, a - 1)
                one_hots(hot_c[:, par, :, :], a * BT, nt).then_inc(c_hot, 1)

            def hot_batch(b, par, nt=BT):
                if not (isinstance(b, int) and b < 2):
                    dve.wait_ge(hot_tr, b - 1)
                    dve.wait_ge(picked_ready, b - 1)
                one_hots(hot[:, par, :, :], b * BT, nt).then_inc(hot_ready, 1)

            BSTEPS = 4

            def place_batch(b, par, slot, n0, nt=BT, nxt=BT, ring_used=True):
                dve.wait_ge(steps_ready, b + 1)
                dve.wait_ge(dve_step, n0)
                v.tensor_copy(steps[0:HI, par, :, 0], runs[0:HI, 1 - par, :, SLOT - 1]).then_inc(dve_step, 1)
                dve.wait_ge(dve_step, n0 + 1)
                flat = lambda a: a[0:HI, par, :, :].rearrange("p a b -> p (a b)")
                v.tensor_tensor_scan(flat(runs), keep[0:HI, :], flat(steps), 0.0, ALU.mult, ALU.add).then_inc(dve_step, 1)
                dve.wait_ge(dve_step, n0 + 2)
                if not (isinstance(b, int) and b < 2):
                    dve.wait_ge(entry_ready, b - 1)
                v.tensor_copy(flat(part1), flat(runs)).then_inc(dve_step, 1)
                dve.wait_ge(dve_step, n0 + 3)
                v.tensor_tensor(flat(part2), flat(runs), flat(part1), ALU.subtract).then_inc(parts_ready, 1)
                if nxt:
                    hot_batch(b + 1, 1 - par, nxt)
                dve.wait_ge(entry_ready, b + 1)
                v.tensor_tensor(picked[:, 0:nt, :], entry_p[:, 0:nt * LO].rearrange("p (t l) -> p t l", l=LO),
                                hot[:, par, 0:nt, HI:P], ALU.mult).then_inc(picked_ready, 1)
                dve.wait_ge(picked_ready, b + 1)
                v.tensor_reduce(base[:, 0:nt], picked[:, 0:nt, :], AX.X, ALU.add).then_inc(dve_step, 1)
                dve.wait_ge(dve_step, n0 + 4)
                dve.wait_ge(rank_ready, b * 2 + 2)
                if ring_used:
                    dve.wait_ge(scattered, b - GB + 1)
                v.tensor_tensor(place[:, slot, 0:nt], base[:, 0:nt], rank[:, par, 0:nt], ALU.add).then_inc(place_ready, 1)

            def split_keys(c0, c1):
                c = slice(c0, c1)
                st.inc(v.tensor_copy(key_f[:, c], key_i[:, c]))
                st.wait(dve)
                st.inc(v.tensor_scalar(hi_f[:, c], key_f[:, c], 1.0 / LO, 0.5 / LO - 0.5, ALU.mult, ALU.add))
                st.wait(dve)
                st.inc(v.tensor_scalar(hi_f[:, c], hi_f[:, c], ROUND, ROUND, ALU.add, ALU.subtract))
                st.wait(dve)
                v.tensor_copy(hi_b[:, c], hi_f[:, c])
                st.inc(v.scalar_tensor_tensor(lo_b[:, c], hi_f[:, c], -float(LO), key_f[:, c], ALU.mult, ALU.add))
                st.wait(dve)

            def early_constants():
                dve.wait_ge(made, 5)
                v.tensor_scalar(keep[:, :], slot_i[:, :], 1.0, None, ALU.min)
                v.tensor_scalar(ident_b[:, :], diff[:, :], 0.0, None, ALU.is_equal)
                v.tensor_scalar(above[:, :], diff[:, :], 0.0, None, ALU.is_gt)
                v.tensor_scalar(ident[:, :], diff[:, :], 0.0, None, ALU.is_equal)
                st.inc(v.tensor_scalar(before[:, :], diff[:, :], 0.0, 3.0, ALU.is_lt, ALU.mult))
                v.memset(ones_lo[:, :], 1.0)
                st.wait(dve)
                v.tensor_scalar(before[:, :], before[:, :], -4.0, None, ALU.add).then_inc(const_ready, 1)

            def late_constants():
                v.tensor_copy(row_f[:, :], row0[:, :])
                v.tensor_copy(ramp[:, :], ramp_i[:, :])
                v.tensor_copy(ramp32[:, :], ramp_i[:, :])
                v.memset(one_row[:, :], 1.0)
                v.memset(cnt_all[:, :], 0.0)
                st.inc(v.memset(limit[:, :], float(M[0])))
                st.wait(dve)
                for s in range(1, NP_ - 1):
                    v.memset(limit[:, s:s + 1], float(M[s]))
                st.inc(v.tensor_scalar(limit[:, NP_ - 1:NP_], row_f[:, :], float(P - 1), -float(PAD), ALU.is_equal, ALU.mult))
                st.wait(dve)
                v.tensor_scalar(limit[:, NP_ - 1:NP_], limit[:, NP_ - 1:NP_], float(M[NP_ - 1]), None, ALU.add).then_inc(const_ready, 1)

            dve.wait_ge(made, 2)
            v.tensor_copy(ramp_b[:, :], ramp_i[:, 0:HI])
            dve.wait_ge(key_first, 16)
            split_keys(0, EARLY)

            started = False
            rings = 0
            for step in PLAN:
                if step[0] == "count":
                    s = step[1]
                    a0, a1, short = batches(s)
                    if s == 1:
                        late_constants()
                        dve.wait_ge(key_loaded, 32)
                        dve.wait_ge(key_tail, 16)
                        split_keys(EARLY, TILES)
                    first_a = a0
                    if s == 0:
                        count_batch(0, 0)
                        count_batch(1, 1)
                        first_a = 2
                    with dve.Fori(first_a // 2, a1 // 2) as q:
                        count_batch(q * 2, 0)
                        count_batch(q * 2 + 1, 1)
                    if short:
                        count_batch(a1, 0, RT)
                        a1 += 1
                    if s == 0:
                        early_constants()
                    dve.wait_ge(c_used, a1)
                    if s >= 1:
                        dve.wait_ge(table_out, 32 * s)
                    st.inc(v.tensor_copy(hist[0:HI, :], hist_p[0:HI, 0:LO]))
                    st.wait(dve)
                    st.inc(v.tensor_tensor_scan(incl[0:HI, :], ones_lo[0:HI, :], hist[0:HI, :], 0.0, ALU.mult, ALU.add))
                    st.wait(dve)
                    st.inc(v.tensor_copy(tot1[0:HI, :], incl[0:HI, LO - 1:LO]))
                    st.wait(dve)
                    v.tensor_tensor(tot2[0:HI, :], incl[0:HI, LO - 1:LO], tot1[0:HI, :], ALU.subtract).then_inc(hist_read, 1)
                    dve.wait_ge(offs_ready, s + 1)
                    st.inc(v.tensor_scalar(ends[0:HI, :], incl[0:HI, :], hist_p[0:HI, 64:65], None, ALU.add))
                    st.wait(dve)
                    v.tensor_tensor(starts[0:HI, s, :], ends[0:HI, :], hist[0:HI, :], ALU.subtract).then_inc(table_ready, 1)
                    dve.wait_ge(table_ready, s + 1)
                elif step[0] == "place":
                    if not started:
                        started = True
                        hot_batch(0, 0)
                    q, q_last = step[1], step[2]
                    if q % HALF == 0 and q // HALF in FIRST_GROUP:
                        st.inc(v.tensor_copy(runs[0:HI, 1, :, SLOT - 1], starts[0:HI, FIRST_GROUP.index(q // HALF), :]))

                    def place_pair(g, k, n0, short_next=False):
                        for par in range(2):
                            place_batch(g * GB + k * 2 + par, par, k * 2 + par, n0 + BSTEPS * par,
                                        nxt=RT if short_next and par else BT, ring_used=not (isinstance(g, int) and g == 0))

                    if q == 0:
                        place_pair(0, 0, st.n)
                        q, st.n = 1, st.n + 2 * BSTEPS
                    short = q_last == N_BATCH // 2
                    q_loops = q_last - short
                    while q < q_loops:
                        g, k = q // HALF, q % HALF
                        if k == 0 and q_loops - q >= HALF:
                            n = (q_loops - q) // HALF
                            with dve.Fori(g, g + n) as gg:
                                with dve.Fori(0, HALF) as kk:
                                    place_pair(gg, kk, gg * (2 * HALF * BSTEPS) + kk * (2 * BSTEPS) + (st.n - g * 2 * HALF * BSTEPS))
                            n *= HALF
                        else:
                            n = min(HALF - k, q_loops - q)
                            with dve.Fori(k, k + n) as kk:
                                place_pair(g, kk, kk * (2 * BSTEPS) + (st.n - k * 2 * BSTEPS))
                        q, st.n = q + n, st.n + 2 * BSTEPS * n
                    if short:
                        place_pair(N_GROUPS - 1, HALF - 1, st.n, short_next=True)
                        st.n += 2 * BSTEPS
                elif step[0] == "rest":
                    place_batch(N_BATCH, 0, 0, st.n, RT, 0)
                    st.n += BSTEPS
                elif step[0] == "heads":
                    s = step[1]
                    dve.wait_ge(table_in, 32 * (s + 1))
                    st.inc(v.tensor_tensor(beg_n[:, :], end_n[:, s, :], cnt_n[:, s, :], ALU.subtract))
                    st.inc(v.tensor_scalar(has_n[:, s, :], cnt_n[:, s, :], 0.0, None, ALU.is_gt))
                    v.tensor_scalar(at_n[:, s, :], end_n[:, s, :], -1.0, 0.0, ALU.add, ALU.max)
                    st.inc(v.tensor_tensor(cnt_all[:, :], cnt_all[:, :], cnt_n[:, s, :], ALU.add))
                    st.wait(dve)
                    st.inc(v.tensor_scalar(hp_n[:, :], beg_n[:, :], 1.0 / M[s], 0.5 / M[s] - 0.5, ALU.mult, ALU.add))
                    st.inc(v.tensor_scalar(cap_n[:, s, :], has_n[:, s, :], 2.0, 1.0, ALU.mult, ALU.subtract))
                    st.wait(dve)
                    st.inc(v.tensor_scalar(hp_n[:, :], hp_n[:, :], ROUND, ROUND, ALU.add, ALU.subtract))
                    st.inc(v.tensor_scalar(cap_n[:, s, :], cap_n[:, s, :], FMAX, None, ALU.mult))
                    st.wait(dve)
                    st.inc(v.scalar_tensor_tensor(hc_n[:, :], hp_n[:, :], -float(M[s]), beg_n[:, :], ALU.mult, ALU.add))
                    st.wait(dve)
                    st.inc(v.scalar_tensor_tensor(hp_n[:, :], has_n[:, s, :], -2.0 * P, hp_n[:, :], ALU.mult, ALU.add))
                    st.wait(dve)
                    st.inc(v.tensor_scalar(hp_n[:, :], hp_n[:, :], 2.0 * P, None, ALU.add))
                    st.wait(dve)
                    for j in range(NODE_J):
                        if j % RING_J == 0 and rings >= 1:
                            dve.wait_ge(heads_used, rings)
                        v.tensor_scalar(head_p[:, j % RING_J, :], ramp[0:NODE_P, 0:P], hp_n[:, j:j + 1], None, ALU.is_equal)
                        ins = v.tensor_scalar(head_c[:, j % RING_J, 0:M[s]], ramp[0:NODE_P, 0:M[s]], hc_n[:, j:j + 1], None,
                                              ALU.is_equal)
                        if j % RING_J == RING_J - 1:
                            rings += 1
                            ins.then_inc(heads_hot, 1)
                    dve.wait_ge(heads_used, rings)
                    m = M[s]
                    st.inc(v.tensor_scalar(whole[:, :], misc_p[:, 0:1], -1.0, 1.0, ALU.mult, ALU.add))
                    v.tensor_scalar(same[:, 0:m], misc_p[:, 0:m], -1.0, 1.0, ALU.mult, ALU.add)
                    st.inc(v.tensor_scalar(far[:, 0:m], misc_p[:, 0:m], -float(MMAX), None, ALU.mult))
                    st.wait(dve)
                    st.inc(v.tensor_copy(links[:, 0, :], whole[:, 0:1].to_broadcast([P, FR])))
                    st.inc(v.memset(same[:, 0:1], 0.0))
                    st.inc(v.tensor_tensor(far[:, 1:m], far[:, 1:m], ramp32[:, 1:m], ALU.add))
                    st.wait(dve)
                    st.inc(v.tensor_reduce(first[:, :], far[:, 1:m], AX.X, ALU.min))
                    st.inc(v.tensor_scalar(cap[:, 0:m], same[:, 0:m], 2.0, 1.0, ALU.mult, ALU.subtract))
                    st.wait(dve)
                    st.inc(v.tensor_scalar(cap[:, 0:m], cap[:, 0:m], FMAX, None, ALU.mult))
                    st.inc(v.tensor_scalar(whole[:, :], first[:, :], 0.5, None, ALU.is_gt))
                    st.inc(v.tensor_scalar(mend_f[:, :], first[:, :], float(MMAX), None, ALU.add))
                    st.wait(dve)
                    st.inc(v.tensor_tensor(mend_f[:, :], mend_f[:, :], limit[:, s:s + 1], ALU.min))
                    st.inc(v.tensor_tensor(links[:, 1, :], links[:, 0, :], whole[:, 0:1].to_broadcast([P, FR]), ALU.mult))
                    st.wait(dve)
                    st.inc(v.scalar_tensor_tensor(mend_f[:, :], row_f[:, :], float(m), mend_f[:, :], ALU.mult, ALU.add))
                    st.wait(dve)
                    st.inc(v.tensor_scalar(mend_at[:, s:s + 1], mend_f[:, :], -1.0, None, ALU.add))
                    st.wait(dve)
                elif step[0] == "scan":
                    s, c = step[1], step[2]
                    k = FIRST_CHUNK[s] + c
                    a, b = CHUNKS[s][c]
                    n = b - a
                    dve.wait_ge(xs_in[k % 2], 16 * (k // 2 + 1))
                    if k >= 2:
                        dve.wait_ge(rs_out[k % 2], 16 * (k // 2))
                    if c:
                        pb = CHUNKS[s][c - 1][1] - CHUNKS[s][c - 1][0] - 1
                        dve.wait_ge(scanned, k)
                    for f in range(FE):
                        before_s = rs[:, (k - 1) % 2, pb, f:f + 1] if c else 0.0
                        before_m = rs[:, (k - 1) % 2, pb, FE + f:FE + f + 1] if c else 0.0
                        v.tensor_tensor_scan(rs[:, k % 2, 0:n, f], same[:, a:b], xs[:, k % 2, 0:n, f],
                                             before_s, ALU.mult, ALU.add)
                        ins = v.tensor_tensor_scan(rs[:, k % 2, 0:n, FE + f], cap[:, a:b], xs[:, k % 2, 0:n, f],
                                                   before_m, ALU.min, ALU.max)
                    ins.then_inc(scanned, 1)
                elif step[0] == "carry":
                    s = step[1]
                    k = FIRST_CHUNK[s + 1] - 1
                    n = CHUNKS[s][-1][1] - CHUNKS[s][-1][0]
                    dve.wait_ge(scanned, k + 1)
                    v.tensor_copy(last[:, :], rs[:, k % 2, n - 1, :]).then_inc(last_ready, 1)
                    dve.wait_ge(tails_ready, s + 1)
                    st.inc(v.tensor_copy(tails[:, :], misc_p[0:FR, 0:P]))
                    st.inc(v.tensor_copy(link_b[:, :], misc_p[0:FR, P:2 * P]))
                    st.inc(v.tensor_copy(link_a[:, :], misc_p[0:FR, 2 * P:3 * P]))
                    st.wait(dve)
                    mx = slice(FE, FR)
                    for t in (link_a, link_b):
                        st.inc(v.tensor_scalar(t[mx, :], t[mx, :], 2.0, 1.0, ALU.mult, ALU.subtract))
                        st.wait(dve)
                        st.inc(v.tensor_scalar(t[mx, :], t[mx, :], FMAX, None, ALU.mult))
                        st.wait(dve)
                    st.inc(v.tensor_tensor_scan(full[0:FE, :], link_a[0:FE, :], tails[0:FE, :], 0.0, ALU.mult, ALU.add))
                    st.inc(v.tensor_tensor_scan(full[mx, :], link_a[mx, :], tails[mx, :], 0.0, ALU.min, ALU.max))
                    st.inc(v.memset(carried[0:FE, 0:1], 0.0))
                    st.inc(v.memset(carried[mx, 0:1], -FMAX))
                    st.wait(dve)
                    v.tensor_tensor(carried[0:FE, 1:P], link_b[0:FE, 1:P], full[0:FE, 0:P - 1], ALU.mult)
                    v.tensor_tensor(carried[mx, 1:P], link_b[mx, 1:P], full[mx, 0:P - 1], ALU.min).then_inc(carried_ready, 1)
                    dve.wait_ge(carry_tr, s + 1)
                    v.tensor_copy(carry[:, :], misc_p[:, 3 * P:3 * P + FR]).then_inc(carry_ready, 1)
                elif step[0] == "mend":
                    s = step[1]
                    dve.wait_ge(mend_in, 16 * (s + 1))
                    dve.wait_ge(carry_ready, s + 1)
                    v.tensor_tensor(mended[:, s, 0:FE], mended[:, s, 0:FE], carry[:, 0:FE], ALU.add)
                    v.tensor_tensor(mended[:, s, FE:FR], mended[:, s, FE:FR], carry[:, FE:FR], ALU.max).then_inc(mend_done, 1)
                elif step[0] == "fetched":
                    s = step[1]
                    dve.wait_ge(fetch_in[s], 16 * NODE_J)
                    shape = [NODE_P, NODE_J, FE]
                    g = got[:, s % 2, :, :]
                    a_sum, a_max = feat[:, :, 0:FE], feat[:, :, FE:2 * FE]
                    m_sum = a_sum if s == 0 else g[:, :, 0:FE]
                    m_max = a_max if s == 0 else g[:, :, FE:FR]
                    ins = v.tensor_tensor(m_sum, g[:, :, 0:FE], has_n[:, s, :].unsqueeze(2).to_broadcast(shape), ALU.mult)
                    if s:
                        st.inc(ins)
                    ins = v.tensor_tensor(m_max, g[:, :, FE:FR], cap_n[:, s, :].unsqueeze(2).to_broadcast(shape), ALU.min)
                    if s:
                        st.inc(ins)
                        st.wait(dve)
                        v.tensor_tensor(a_sum, a_sum, m_sum, ALU.add)
                        ins = v.tensor_tensor(a_max, a_max, m_max, ALU.max)
                    ins.then_inc(got_used, 1)
                    dve.wait_ge(got_used, s + 1)
                    if s == NP_ - 2:
                        st.inc(v.tensor_scalar(cnt_1[:, :], cnt_all[:, :], 1.0, None, ALU.max))
                        st.inc(v.tensor_scalar(has_all[:, :], cnt_all[:, :], 1.0, None, ALU.min))
                        st.wait(dve)
                        st.inc(v.reciprocal(inv[:, :], cnt_1[:, :]))
                        for par in range(2):
                            dve.wait_ge(rs_out[par], 16 * len([k for k in range(FIRST_CHUNK[-1]) if k % 2 == par]))
                        dve.wait_ge(bias_p, 2)
                        dve.wait_ge(h_ready, 1)
                        dve.wait_ge(x_loaded, 16)
                        st.inc(v.tensor_tensor(x_s[:, :, :], x_s[:, :, :],
                                               hist_p[0:NODE_P, 128:128 + FN].unsqueeze(1).to_broadcast([NODE_P, NODE_J, FN]),
                                               ALU.add))
            for k in range(NB + 4):
                if k < NB:
                    a, b = blocks[k]
                    sh = [NODE_P, b - a, FE]
                    s = NP_ - 1
                    g = got[:, s % 2, a:b, :]
                    wide = lambda t: t[:, a:b].unsqueeze(2).to_broadcast(sh)
                    dve.wait_ge(fetch_last[k], 16 * (b - a))
                    st.inc(v.tensor_tensor(g[:, :, 0:FE], g[:, :, 0:FE], wide(has_n[:, s, :]), ALU.mult))
                    st.inc(v.tensor_tensor(g[:, :, FE:FR], g[:, :, FE:FR], wide(cap_n[:, s, :]), ALU.min))
                    st.wait(dve)
                    st.inc(v.tensor_tensor(feat[:, a:b, 0:FE], feat[:, a:b, 0:FE], g[:, :, 0:FE], ALU.add))
                    st.inc(v.tensor_tensor(feat[:, a:b, FE:2 * FE], feat[:, a:b, FE:2 * FE], g[:, :, FE:FR], ALU.max))
                    st.wait(dve)
                    v.tensor_tensor(feat[:, a:b, 2 * FE:3 * FE], feat[:, a:b, 0:FE], wide(inv), ALU.mult)
                    v.tensor_tensor(feat[:, a:b, FE:2 * FE], feat[:, a:b, FE:2 * FE], wide(has_all), ALU.mult).then_inc(feat_ready, 1)
                if 0 <= k - 4 < NB:
                    q = k - 4
                    a, b = blocks[q]
                    dve.wait_ge(std_ready, q + 1)
                    st.inc(v.reciprocal(rstd[:, a:b], std[:, a:b]))
                    dve.wait_ge(centred, q + 1)
                    st.wait(dve)
                    v.tensor_tensor(o_s[:, a:b, :], y[:, a:b, :], rstd[:, a:b].unsqueeze(2).to_broadcast([NODE_P, b - a, FN]),
                                    ALU.mult).then_inc(o_ready, 1)
                if 0 <= k - 3 < NB:
                    a, b = blocks[k - 3]
                    dve.wait_ge(sq_ready, k - 2)
                    st.inc(v.tensor_reduce(var[:, a:b], sq[:, a:b, :], AX.X, ALU.add))
                    st.wait(dve)
                    v.tensor_scalar(var[:, a:b], var[:, a:b], 1.0 / FN, EPS, ALU.mult, ALU.add).then_inc(var_ready, 1)
                if 0 <= k - 2 < NB:
                    q = k - 2
                    a, b = blocks[q]
                    dve.wait_ge(y_p, q + 1)
                    st.inc(v.tensor_tensor(y[:, a:b, :], x_s[:, a:b, :],
                                           [steps_p, entry_p][q % 2][0:NODE_P, 0:(b - a) * FN].rearrange("p (a b) -> p a b", b=FN),
                                           ALU.add))
                    st.wait(dve)
                    st.inc(v.tensor_reduce(mean[:, a:b], y[:, a:b, :], AX.X, ALU.add))
                    st.wait(dve)
                    v.scalar_tensor_tensor(y[:, a:b, :], mean[:, a:b].unsqueeze(2).to_broadcast([NODE_P, b - a, FN]), -1.0 / FN,
                                           y[:, a:b, :], ALU.mult, ALU.add).then_inc(centred, 1)


_INS = ["x", "src", "edge_attr_32", "L0_gnn_u", "L0_gnn_W1", "L0_gnn_b1", "L0_gnn_W2", "L0_gnn_b2"]


def kernel(**inputs):
    import numpy as _np
    import concourse.bacc as _bacc
    from concourse import mybir as _mybir
    from concourse.bass_utils import run_bass_kernel_spmd as _run

    nc = _bacc.Bacc("TRN2", target_bir_lowering=False, num_devices=1)
    arrays, args = {}, []
    for name in _INS:
        a = _np.ascontiguousarray(inputs[name])
        arrays[f"in_{name}"] = a
        args.append(nc.dram_tensor(f"in_{name}", a.shape, _mybir.dt.from_np(a.dtype), kind="ExternalInput").ap())
    out = nc.dram_tensor("out_nodes", (N_NODES, FN), _mybir.dt.from_np(_np.dtype("float32")), kind="ExternalOutput").ap()
    gnn_kernel(nc, *args, out)
    r = _run(nc, [arrays], core_ids=[0])
    return r.results[0]["out_nodes"]
```
